# Optimizing a Trainium2 kernel written in Bass

```python
import numpy as np
import jax
import jax.numpy as jnp

def _softmax(x, axis=-1):
    return jax.nn.softmax(x, axis=axis)

def _gelu(x):
    return jax.nn.gelu(x, approximate=True)

def _silu(x):
    return jax.nn.silu(x)

def _sigmoid(x):
    return jax.nn.sigmoid(x)

def _layernorm(x, axis=-1, eps=1e-05):
    m = jnp.mean(x, axis=axis, keepdims=True)
    v = jnp.var(x, axis=axis, keepdims=True)
    return (x - m) / jnp.sqrt(v + eps)

def _scatter_add(tgt, idx, src, axis=0):
    return tgt.at[idx].add(src)

def _segment_sum(src, seg, n):
    return jax.ops.segment_sum(src, seg, n)
kernel_name = 'mk_dlrm_tower_d1_rec_r8_64d8f0'

def setup_inputs(seed: int=0):
    np.random.seed(seed)
    _w = jnp.asarray

    def _rec_inputs():
        import jax
        import jax.numpy as jnp
        _tk = jax.random.key(seed)
        dense_ctx = jax.random.normal(jax.random.fold_in(_tk, 190), (512, 16), jnp.float32)
        ids = jnp.stack([jax.random.randint(jax.random.fold_in(_tk, 200 + f), (512,), 0, v, jnp.int32) for f, v in enumerate([125000, 1250, 1000, 1000, 1000, 1250, 12500, 1000, 1250, 12500, 1250, 125000, 1000, 1000, 1000, 1250, 1250, 125000, 125000, 125000, 12500, 1000, 125000, 1250, 125000, 125000, 125000, 12500, 12500, 125000, 125000, 1000, 1000, 12500, 125000, 125000, 125000, 1000, 1250])], axis=1)
        tbl_0 = 0.05 * jax.random.normal(jax.random.fold_in(_tk, 500 + 0), (125000, 16), jnp.float32)
        tbl_1 = 0.05 * jax.random.normal(jax.random.fold_in(_tk, 500 + 1), (1250, 16), jnp.float32)
        tbl_2 = 0.05 * jax.random.normal(jax.random.fold_in(_tk, 500 + 2), (1000, 16), jnp.float32)
        tbl_3 = 0.05 * jax.random.normal(jax.random.fold_in(_tk, 500 + 3), (1000, 16), jnp.float32)
        tbl_4 = 0.05 * jax.random.normal(jax.random.fold_in(_tk, 500 + 4), (1000, 16), jnp.float32)
        tbl_5 = 0.05 * jax.random.normal(jax.random.fold_in(_tk, 500 + 5), (1250, 16), jnp.float32)
        tbl_6 = 0.05 * jax.random.normal(jax.random.fold_in(_tk, 500 + 6), (12500, 16), jnp.float32)
        tbl_7 = 0.05 * jax.random.normal(jax.random.fold_in(_tk, 500 + 7), (1000, 16), jnp.float32)
        tbl_8 = 0.05 * jax.random.normal(jax.random.fold_in(_tk, 500 + 8), (1250, 16), jnp.float32)
        tbl_9 = 0.05 * jax.random.normal(jax.random.fold_in(_tk, 500 + 9), (12500, 16), jnp.float32)
        tbl_10 = 0.05 * jax.random.normal(jax.random.fold_in(_tk, 500 + 10), (1250, 16), jnp.float32)
        tbl_11 = 0.05 * jax.random.normal(jax.random.fold_in(_tk, 500 + 11), (125000, 16), jnp.float32)
        tbl_12 = 0.05 * jax.random.normal(jax.random.fold_in(_tk, 500 + 12), (1000, 16), jnp.float32)
        tbl_13 = 0.05 * jax.random.normal(jax.random.fold_in(_tk, 500 + 13), (1000, 16), jnp.float32)
        tbl_14 = 0.05 * jax.random.normal(jax.random.fold_in(_tk, 500 + 14), (1000, 16), jnp.float32)
        tbl_15 = 0.05 * jax.random.normal(jax.random.fold_in(_tk, 500 + 15), (1250, 16), jnp.float32)
        tbl_16 = 0.05 * jax.random.normal(jax.random.fold_in(_tk, 500 + 16), (1250, 16), jnp.float32)
        tbl_17 = 0.05 * jax.random.normal(jax.random.fold_in(_tk, 500 + 17), (125000, 16), jnp.float32)
        tbl_18 = 0.05 * jax.random.normal(jax.random.fold_in(_tk, 500 + 18), (125000, 16), jnp.float32)
        tbl_19 = 0.05 * jax.random.normal(jax.random.fold_in(_tk, 500 + 19), (125000, 16), jnp.float32)
        tbl_20 = 0.05 * jax.random.normal(jax.random.fold_in(_tk, 500 + 20), (12500, 16), jnp.float32)
        tbl_21 = 0.05 * jax.random.normal(jax.random.fold_in(_tk, 500 + 21), (1000, 16), jnp.float32)
        tbl_22 = 0.05 * jax.random.normal(jax.random.fold_in(_tk, 500 + 22), (125000, 16), jnp.float32)
        tbl_23 = 0.05 * jax.random.normal(jax.random.fold_in(_tk, 500 + 23), (1250, 16), jnp.float32)
        tbl_24 = 0.05 * jax.random.normal(jax.random.fold_in(_tk, 500 + 24), (125000, 16), jnp.float32)
        tbl_25 = 0.05 * jax.random.normal(jax.random.fold_in(_tk, 500 + 25), (125000, 16), jnp.float32)
        tbl_26 = 0.05 * jax.random.normal(jax.random.fold_in(_tk, 500 + 26), (125000, 16), jnp.float32)
        tbl_27 = 0.05 * jax.random.normal(jax.random.fold_in(_tk, 500 + 27), (12500, 16), jnp.float32)
        tbl_28 = 0.05 * jax.random.normal(jax.random.fold_in(_tk, 500 + 28), (12500, 16), jnp.float32)
        tbl_29 = 0.05 * jax.random.normal(jax.random.fold_in(_tk, 500 + 29), (125000, 16), jnp.float32)
        tbl_30 = 0.05 * jax.random.normal(jax.random.fold_in(_tk, 500 + 30), (125000, 16), jnp.float32)
        tbl_31 = 0.05 * jax.random.normal(jax.random.fold_in(_tk, 500 + 31), (1000, 16), jnp.float32)
        tbl_32 = 0.05 * jax.random.normal(jax.random.fold_in(_tk, 500 + 32), (1000, 16), jnp.float32)
        tbl_33 = 0.05 * jax.random.normal(jax.random.fold_in(_tk, 500 + 33), (12500, 16), jnp.float32)
        tbl_34 = 0.05 * jax.random.normal(jax.random.fold_in(_tk, 500 + 34), (125000, 16), jnp.float32)
        tbl_35 = 0.05 * jax.random.normal(jax.random.fold_in(_tk, 500 + 35), (125000, 16), jnp.float32)
        tbl_36 = 0.05 * jax.random.normal(jax.random.fold_in(_tk, 500 + 36), (125000, 16), jnp.float32)
        tbl_37 = 0.05 * jax.random.normal(jax.random.fold_in(_tk, 500 + 37), (1000, 16), jnp.float32)
        tbl_38 = 0.05 * jax.random.normal(jax.random.fold_in(_tk, 500 + 38), (1250, 16), jnp.float32)
        _rk = jax.random.fold_in(_tk, 7)
        W_top1 = 0.0606339 * jax.random.normal(jax.random.fold_in(_tk, 801), (272, 512), jnp.float32)
        W_top2 = 0.0441942 * jax.random.normal(jax.random.fold_in(_tk, 802), (512, 256), jnp.float32)
        W_top3 = 0.0625 * jax.random.normal(jax.random.fold_in(_tk, 803), (256, 1), jnp.float32)
        b_top1 = jnp.zeros((512,), jnp.float32)
        b_top2 = jnp.zeros((256,), jnp.float32)
        return (dense_ctx, ids, tbl_0, tbl_1, tbl_2, tbl_3, tbl_4, tbl_5, tbl_6, tbl_7, tbl_8, tbl_9, tbl_10, tbl_11, tbl_12, tbl_13, tbl_14, tbl_15, tbl_16, tbl_17, tbl_18, tbl_19, tbl_20, tbl_21, tbl_22, tbl_23, tbl_24, tbl_25, tbl_26, tbl_27, tbl_28, tbl_29, tbl_30, tbl_31, tbl_32, tbl_33, tbl_34, tbl_35, tbl_36, tbl_37, tbl_38, W_top1, b_top1, W_top2, b_top2, W_top3)
    dense_ctx, ids, tbl_0, tbl_1, tbl_2, tbl_3, tbl_4, tbl_5, tbl_6, tbl_7, tbl_8, tbl_9, tbl_10, tbl_11, tbl_12, tbl_13, tbl_14, tbl_15, tbl_16, tbl_17, tbl_18, tbl_19, tbl_20, tbl_21, tbl_22, tbl_23, tbl_24, tbl_25, tbl_26, tbl_27, tbl_28, tbl_29, tbl_30, tbl_31, tbl_32, tbl_33, tbl_34, tbl_35, tbl_36, tbl_37, tbl_38, W_top1, b_top1, W_top2, b_top2, W_top3 = _rec_inputs()

    def _L0_rec_setup():
        import jax, jax.numpy as jnp
        import numpy as np
        B, F0, D = (256, 39, 16)
        LAYER_SIZES = [128, 128, 128]
        key = jax.random.key(seed)
        ks = jax.random.split(key, 1 + 2 * len(LAYER_SIZES))
        inputs = jax.random.normal(ks[0], (B, F0, D), dtype=jnp.float32)
        out = {'inputs': inputs}
        field_nums = [F0]
        for i, size in enumerate(LAYER_SIZES):
            fk = field_nums[-1]
            fan_in = F0 * fk
            scale = np.sqrt(2.0 / (fan_in + size)).astype(np.float32)
            out[f'w{i}'] = jax.random.normal(ks[1 + 2 * i], (F0, fk, size), dtype=jnp.float32) * scale
            out[f'b{i}'] = jnp.zeros((size,), dtype=jnp.float32)
            field_nums.append(size // 2)
        return out
    _L0_rec_all = _L0_rec_setup()
    _L0_rec_in = {k: v for k, v in _L0_rec_all.items() if k in ('w0', 'w1', 'w2', 'b0', 'b1', 'b2')}
    del _L0_rec_all
    return {'dense_ctx': dense_ctx, 'ids': ids, 'tbl_0': tbl_0, 'tbl_1': tbl_1, 'tbl_2': tbl_2, 'tbl_3': tbl_3, 'tbl_4': tbl_4, 'tbl_5': tbl_5, 'tbl_6': tbl_6, 'tbl_7': tbl_7, 'tbl_8': tbl_8, 'tbl_9': tbl_9, 'tbl_10': tbl_10, 'tbl_11': tbl_11, 'tbl_12': tbl_12, 'tbl_13': tbl_13, 'tbl_14': tbl_14, 'tbl_15': tbl_15, 'tbl_16': tbl_16, 'tbl_17': tbl_17, 'tbl_18': tbl_18, 'tbl_19': tbl_19, 'tbl_20': tbl_20, 'tbl_21': tbl_21, 'tbl_22': tbl_22, 'tbl_23': tbl_23, 'tbl_24': tbl_24, 'tbl_25': tbl_25, 'tbl_26': tbl_26, 'tbl_27': tbl_27, 'tbl_28': tbl_28, 'tbl_29': tbl_29, 'tbl_30': tbl_30, 'tbl_31': tbl_31, 'tbl_32': tbl_32, 'tbl_33': tbl_33, 'tbl_34': tbl_34, 'tbl_35': tbl_35, 'tbl_36': tbl_36, 'tbl_37': tbl_37, 'tbl_38': tbl_38, 'W_top1': W_top1, 'b_top1': b_top1, 'W_top2': W_top2, 'b_top2': b_top2, 'W_top3': W_top3, 'L0_rec_w0': _L0_rec_in['w0'], 'L0_rec_w1': _L0_rec_in['w1'], 'L0_rec_w2': _L0_rec_in['w2'], 'L0_rec_b0': _L0_rec_in['b0'], 'L0_rec_b1': _L0_rec_in['b1'], 'L0_rec_b2': _L0_rec_in['b2']}

def reference(dense_ctx, ids, tbl_0, tbl_1, tbl_2, tbl_3, tbl_4, tbl_5, tbl_6, tbl_7, tbl_8, tbl_9, tbl_10, tbl_11, tbl_12, tbl_13, tbl_14, tbl_15, tbl_16, tbl_17, tbl_18, tbl_19, tbl_20, tbl_21, tbl_22, tbl_23, tbl_24, tbl_25, tbl_26, tbl_27, tbl_28, tbl_29, tbl_30, tbl_31, tbl_32, tbl_33, tbl_34, tbl_35, tbl_36, tbl_37, tbl_38, W_top1, b_top1, W_top2, b_top2, W_top3, L0_rec_w0, L0_rec_w1, L0_rec_w2, L0_rec_b0, L0_rec_b1, L0_rec_b2):
    import jax
    import jax.numpy as jnp

    def _L0_rec_ref(inputs, w0, w1, w2, b0, b1, b2):
        import jax, jax.numpy as jnp
        import numpy as np
        B, F0, D = (256, 39, 16)
        LAYER_SIZES = [128, 128, 128]
        x0 = inputs
        xk = inputs
        params = [(w0, b0), (w1, b1), (w2, b2)]
        n_layers = len(params)
        direct = []
        for idx, (W, b) in enumerate(params):
            z = jnp.einsum('bhd,bkd,hks->bsd', x0, xk, W) + b[None, :, None]
            z = jax.nn.relu(z)
            if idx != n_layers - 1:
                half = z.shape[1] // 2
                xk = z[:, :half, :]
                direct.append(z[:, half:, :])
            else:
                direct.append(z)
        logit = jnp.sum(jnp.concatenate(direct, axis=1), axis=-1)
        return logit
    e = jnp.stack([tbl_0[ids[:, 0]], tbl_1[ids[:, 1]], tbl_2[ids[:, 2]], tbl_3[ids[:, 3]], tbl_4[ids[:, 4]], tbl_5[ids[:, 5]], tbl_6[ids[:, 6]], tbl_7[ids[:, 7]], tbl_8[ids[:, 8]], tbl_9[ids[:, 9]], tbl_10[ids[:, 10]], tbl_11[ids[:, 11]], tbl_12[ids[:, 12]], tbl_13[ids[:, 13]], tbl_14[ids[:, 14]], tbl_15[ids[:, 15]], tbl_16[ids[:, 16]], tbl_17[ids[:, 17]], tbl_18[ids[:, 18]], tbl_19[ids[:, 19]], tbl_20[ids[:, 20]], tbl_21[ids[:, 21]], tbl_22[ids[:, 22]], tbl_23[ids[:, 23]], tbl_24[ids[:, 24]], tbl_25[ids[:, 25]], tbl_26[ids[:, 26]], tbl_27[ids[:, 27]], tbl_28[ids[:, 28]], tbl_29[ids[:, 29]], tbl_30[ids[:, 30]], tbl_31[ids[:, 31]], tbl_32[ids[:, 32]], tbl_33[ids[:, 33]], tbl_34[ids[:, 34]], tbl_35[ids[:, 35]], tbl_36[ids[:, 36]], tbl_37[ids[:, 37]], tbl_38[ids[:, 38]]], axis=1)
    z = _L0_rec_ref(e, L0_rec_w0, L0_rec_w1, L0_rec_w2, L0_rec_b0, L0_rec_b1, L0_rec_b2)
    z = z.reshape(z.shape[0], -1)
    h = jnp.concatenate([z, dense_ctx], axis=1)
    h = jnp.maximum(h @ W_top1 + b_top1, 0.0)
    h = jnp.maximum(h @ W_top2 + b_top2, 0.0)
    y = h @ W_top3
    return y

_drawn_inputs = setup_inputs


def setup_inputs(seed=0):
    import zlib

    import numpy as np

    out = dict(_drawn_inputs(seed))
    spreads = {'b_top1': (0.0, 2.0),
     'b_top2': (0.0, 2.0),
     'L0_rec_b0': (0.0, 0.342),
     'L0_rec_b1': (0.0, 0.547),
     'L0_rec_b2': (0.0, 0.8)}
    factors = {'tbl_0': 8.0,
     'tbl_1': 8.0,
     'tbl_2': 8.0,
     'tbl_3': 8.0,
     'tbl_4': 8.0,
     'tbl_5': 8.0,
     'tbl_6': 8.0,
     'tbl_7': 8.0,
     'tbl_8': 8.0,
     'tbl_9': 8.0,
     'tbl_10': 8.0,
     'tbl_11': 8.0,
     'tbl_12': 8.0,
     'tbl_13': 8.0,
     'tbl_14': 8.0,
     'tbl_15': 8.0,
     'tbl_16': 8.0,
     'tbl_17': 8.0,
     'tbl_18': 8.0,
     'tbl_19': 8.0,
     'tbl_20': 8.0,
     'tbl_21': 8.0,
     'tbl_22': 8.0,
     'tbl_23': 8.0,
     'tbl_24': 8.0,
     'tbl_25': 8.0,
     'tbl_26': 8.0,
     'tbl_27': 8.0,
     'tbl_28': 8.0,
     'tbl_29': 8.0,
     'tbl_30': 8.0,
     'tbl_31': 8.0,
     'tbl_32': 8.0,
     'tbl_33': 8.0,
     'tbl_34': 8.0,
     'tbl_35': 8.0,
     'tbl_36': 8.0,
     'tbl_37': 8.0,
     'tbl_38': 8.0,
     'L0_rec_w0': 8.0,
     'L0_rec_w1': 6.31,
     'L0_rec_w2': 4.648,
     'dense_ctx': 8.0}
    for name, (base, spread) in spreads.items():
        noise = np.random.default_rng([zlib.crc32(name.encode()), seed]).standard_normal(out[name].shape)
        drawn = base * np.exp(spread * noise) if base else spread * noise
        out[name] = jnp.asarray(drawn.astype(out[name].dtype))
    for name, factor in factors.items():
        out[name] = (out[name] * factor).astype(out[name].dtype)
    return out
```

```python
from contextlib import ExitStack

import numpy as np

import concourse.bass as bass
from concourse import mybir

F32 = mybir.dt.float32
F32R = mybir.dt.float32r
I32 = mybir.dt.int32
ALU = mybir.AluOpType
ACT = mybir.ActivationFunctionType
AX = mybir.AxisListType

P = 128
BATCH, FIELDS, DIM = 512, 39, 16
VOCABS = [125000, 1250, 1000, 1000, 1000, 1250, 12500, 1000, 1250, 12500, 1250, 125000, 1000, 1000,
          1000, 1250, 1250, 125000, 125000, 125000, 12500, 1000, 125000, 1250, 125000, 125000,
          125000, 12500, 12500, 125000, 125000, 1000, 1000, 12500, 125000, 125000, 125000, 1000, 1250]
LAYER = 128
HALF = LAYER // 2
N = 512
TB = N // DIM
TILES = BATCH // TB
GP, GJ = 104, FIELDS * TB // 104
OFFSETS = FIELDS // 2 + 1
OPC = P // FIELDS
ROWS0 = OPC * FIELDS
CHUNKS0 = -(-OFFSETS // OPC)
LAST0 = (OFFSETS - OPC * (CHUNKS0 - 1)) * FIELDS
CHUNKS = -(-FIELDS // 2)
GROUP = 4
RING = 4
GROUPS0 = [(0, 4, 1), (4, 3, 1)]
GROUPS12 = [(4 * g, 4, s) for g, s in enumerate((2, 1, 2, 1, 2))]
G0, G12 = len(GROUPS0), len(GROUPS12)
PER_TILE = G0 + 2 * G12
MAX_SPLIT = 2
H1, H2 = 512, 256


def build(nc, tables, ids, field_base, w0, w0_mirror, w1, w2, cin_bias, dense, wt1, bt1, wt2, bt2,
          wt3, y):
    x0_dram = nc.dram_tensor("x0_scratch", (TILES, 2, FIELDS, N), F32, kind="Internal").ap()

    with ExitStack() as ctx:
        def sb(name, shape, dt=F32):
            return ctx.enter_context(nc.sbuf_tensor(name, shape, dt))

        def sem(name):
            return ctx.enter_context(nc.semaphore(name))

        ids_sb = sb("ids_sb", [GP, TILES * GJ], I32)
        base_sb = sb("base_sb", [GP, GJ], I32)
        rows_now = sb("rows_now", [GP, 2, GJ], I32)
        gathered = sb("gathered", [GP, 2, GJ * DIM])
        x0_pairs = sb("x0_pairs", [P, CHUNKS, N])
        x0_shifted = sb("x0_shifted", [P, CHUNKS0, N])
        x0_thrice = sb("x0_thrice", [P, N])
        x1 = sb("x1", [P, N])
        x2 = sb("x2", [P, N])
        direct01 = sb("direct01", [P, N])
        direct2 = sb("direct2", [P, N])
        prod = sb("prod", [P, RING, GROUP, N])
        prod_hi = sb("prod_hi", [P, RING, MAX_SPLIT, N], F32R)
        prod_lo = sb("prod_lo", [P, RING, MAX_SPLIT, N], F32R)
        w0_sb = sb("w0_sb", [P, CHUNKS0, LAYER])
        w0m_sb = sb("w0m_sb", [P, CHUNKS0, LAYER])
        w1_sb = sb("w1_sb", [P, CHUNKS, LAYER])
        w2_sb = sb("w2_sb", [P, CHUNKS, LAYER])

        def split_index(groups):
            chunks = [c0 + i for c0, _, s in groups for i in range(s)]
            return {c: i for i, c in enumerate(chunks)}

        SPLIT0, SPLIT12 = split_index(GROUPS0), split_index(GROUPS12)
        w0_hi = sb("w0_hi", [P, len(SPLIT0), LAYER], F32R)
        w0_lo = sb("w0_lo", [P, len(SPLIT0), LAYER], F32R)
        w1_hi = sb("w1_hi", [P, len(SPLIT12), LAYER], F32R)
        w1_lo = sb("w1_lo", [P, len(SPLIT12), LAYER], F32R)
        w2_hi = sb("w2_hi", [P, len(SPLIT12), LAYER], F32R)
        w2_lo = sb("w2_lo", [P, len(SPLIT12), LAYER], F32R)
        bias = sb("bias", [P, 3])
        logits = sb("logits", [P, 2, BATCH])
        dense_sb = sb("dense_sb", [DIM, BATCH])
        wt1_sb = sb("wt1_sb", [P, 2, H1])
        wt1d_sb = sb("wt1d_sb", [DIM, H1])
        wt2_sb = sb("wt2_sb", [P, H1 // P, H2])
        wt3_sb = sb("wt3_sb", [P, H2 // P])
        bt1_sb = sb("bt1_sb", [P, H1 // P])
        bt2_sb = sb("bt2_sb", [P, H2 // P])
        y_sb = sb("y_sb", [1, BATCH])
        h1 = prod[:, 0]
        h2 = prod[:, 1, 0:H2 // P]

        acc = [ctx.enter_context(nc.psum_tensor(f"acc{i}", [P, N], F32)) for i in range(3)]
        acc_h1 = ctx.enter_context(nc.psum_tensor("acc_h1", [P, H1 // P, BATCH], F32))
        acc_h2 = acc[0:H2 // P]
        acc_y = acc[2]

        ids_loaded = sem("ids_loaded")
        w0_loaded = sem("w0_loaded")
        bias_loaded = sem("bias_loaded")
        w1_loaded = sem("w1_loaded")
        w2_loaded = sem("w2_loaded")
        mlp_loaded = sem("mlp_loaded")
        row_ids = sem("row_ids")
        rows_in = sem("rows_in")
        x0_stored = [sem(f"x0_stored{i}") for i in range(2)]
        shifted_in = sem("shifted_in")
        pairs_in = [sem(f"pairs_in{g}") for g in range(G12)]
        w0_added = sem("w0_added")
        w_rounded = sem("w_rounded")
        w_split = sem("w_split")
        prod_ready = sem("prod_ready")
        hi_ready = sem("hi_ready")
        lo_ready = sem("lo_ready")
        contracted = sem("contracted")
        x1_ready = sem("x1_ready")
        acc0_read = sem("acc0_read")
        x2_ready = sem("x2_ready")
        acc1_read = sem("acc1_read")
        acc2_read = sem("acc2_read")
        sum01_done = sem("sum01_done")
        sum2_done = sem("sum2_done")
        h1_ready, h1_relu, h2_ready, h2_relu = sem("h1_ready"), sem("h1_relu"), sem("h2_ready"), sem("h2_relu")
        y_ready, y_copied, y_stored = sem("y_ready"), sem("y_copied"), sem("y_stored")

        def before(eng, t):
            return G0 + PER_TILE * t if isinstance(t, int) else eng.snap(t * PER_TILE + G0)

        def buffer(g):
            return g % RING

        assert PER_TILE % RING == 0

        block = ctx.enter_context(nc.Block())

        @block.sync
        def _(sp):
            def load_shifted(t):
                a = x0_dram[t, 0]
                tile = a.offset
                sp.dma_start(x0_thrice[0:ROWS0, :],
                             bass.AP(tensor=a.tensor, offset=tile, ap=[[0, OPC], [N, FIELDS], [1, N]])
                             ).then_inc(shifted_in, 16)
                for o in range(OPC):
                    sp.dma_start(x0_shifted[o * FIELDS:(o + 1) * FIELDS, :, :],
                                 bass.AP(tensor=a.tensor, offset=tile + o * N,
                                         ap=[[N, FIELDS], [OPC * N, CHUNKS0], [1, N]])
                                 ).then_inc(shifted_in, 16)

            def load_pairs(t, g):
                c, n, _ = GROUPS12[g]
                a = x0_dram[t, 0]
                for i in range(2):
                    sp.dma_start(x0_pairs[i * HALF:(i + 1) * HALF, c:c + n, :],
                                 bass.AP(tensor=a.tensor, offset=a.offset + (2 * c + i) * N,
                                         ap=[[0, HALF], [2 * N, n], [1, N]])
                                 ).then_inc(pairs_in[g], 16)

            sp.wait_ge(x0_stored[0], 32)
            load_shifted(0)
            for g in range(G12):
                load_pairs(0, g)
            sp.wait_ge(x0_stored[1], 32)
            sp.wait_ge(prod_ready, G0)
            load_shifted(1)

            with sp.Fori(0, (TILES - 2) // 2) as u:
                n = sp.snap(u * (2 * PER_TILE) + G0)
                stored = sp.snap(u * 32)
                for odd in range(2):
                    t = sp.snap(u * 2 + odd)
                    for g in range(G12):
                        sp.wait_ge(prod_ready, n + (PER_TILE * odd + G12 + G0 + g + 1))
                        load_pairs(sp.snap(t + 1), g)
                    sp.wait_ge(x0_stored[odd], stored + 64)
                    load_shifted(sp.snap(t + 2))
            n = before(sp, TILES - 2)
            for g in range(G12):
                sp.wait_ge(prod_ready, n + G12 + G0 + g + 1)
                load_pairs(TILES - 1, g)

        @block.gpsimd
        def _(pool):
            pool.dma_start(ids_sb[:, :].rearrange("p (t j) -> p t j", j=GJ),
                           ids.rearrange("t (p j) -> p t j", j=GJ)).then_inc(ids_loaded, 16)
            pool.dma_start(base_sb[:, :], field_base).then_inc(ids_loaded, 16)
            pool.wait_ge(ids_loaded, 32)

            def gather(t, odd, n_rows, n_stored):
                pool.tensor_tensor(rows_now[:, odd, :], ids_sb[:, bass.ds(t * GJ, GJ)], base_sb[:, :],
                                   ALU.add).then_inc(row_ids, 1)
                pool.wait_ge(row_ids, 1)
                pool.sem_clear(row_ids)
                for j in range(GJ):
                    pool.indirect_dma_start(
                        gathered[:, odd, j * DIM:(j + 1) * DIM], None, tables,
                        bass.IndirectOffsetOnAxis(ap=rows_now[:, odd, j:j + 1], axis=0)
                    ).then_inc(rows_in, 16)
                pool.wait_ge(rows_in, n_rows + 16 * GJ)
                for copy in range(2):
                    pool.dma_start(x0_dram[t, copy].rearrange("f (b d) -> (f b d)", d=DIM)
                                   .rearrange("(p m) -> p m", p=GP),
                                   gathered[:, odd, :]).then_inc(x0_stored[odd], 16)

            for t in range(2):
                gather(t, t, 16 * GJ * t, 0)
            with pool.Fori(1, TILES // 2) as u:
                n_rows = pool.snap(u * (32 * GJ))
                n_stored = pool.snap(u * 32)
                for odd in range(2):
                    pool.wait_ge(x0_stored[odd], n_stored)
                    gather(pool.snap(u * 2 + odd), odd, n_rows + 16 * GJ * odd, n_stored)
            for odd in range(2):
                pool.wait_ge(x0_stored[odd], 32 * (TILES // 2))

        @block.scalar
        def _(act):
            act.dma_start(w0_sb[0:ROWS0, :, :], w0.rearrange("(c p) s -> p c s", p=ROWS0)).then_inc(w0_loaded, 16)
            act.dma_start(w0m_sb[0:ROWS0, :, :], w0_mirror.rearrange("(c p) s -> p c s", p=ROWS0)).then_inc(w0_loaded, 16)
            act.dma_start(bias[:, :], cin_bias).then_inc(bias_loaded, 16)
            for w, w_sb, loaded in ((w1, w1_sb, w1_loaded), (w2, w2_sb, w2_loaded)):
                whole = (CHUNKS - 1) * P
                act.dma_start(w_sb[:, 0:CHUNKS - 1, :], w[0:whole, :].rearrange("(c p) s -> p c s", p=P)).then_inc(loaded, 16)
                act.dma_start(w_sb[0:HALF, CHUNKS - 1, :], w[whole:, :]).then_inc(loaded, 16)
            act.dma_start(dense_sb[:, :], dense).then_inc(mlp_loaded, 16)
            act.dma_start(wt1_sb[:, :, :], wt1[0:2 * P, :].rearrange("(c p) n -> p c n", p=P)).then_inc(mlp_loaded, 16)
            act.dma_start(wt1d_sb[:, :], wt1[2 * P:, :]).then_inc(mlp_loaded, 16)
            act.dma_start(wt2_sb[:, :, :], wt2.rearrange("(c p) n -> p c n", p=P)).then_inc(mlp_loaded, 16)
            act.dma_start(wt3_sb[:, :], wt3).then_inc(mlp_loaded, 16)
            act.dma_start(bt1_sb[:, :], bt1).then_inc(mlp_loaded, 16)
            act.dma_start(bt2_sb[:, :], bt2).then_inc(mlp_loaded, 16)

            act.wait_ge(w0_added, 1)
            for c, i in SPLIT0.items():
                last = nc.scalar.copy(w0_hi[0:ROWS0, i, :], w0_sb[0:ROWS0, c, :])
            last.then_inc(w_rounded, 1)
            for w_sb, w_hi, loaded in ((w1_sb, w1_hi, w1_loaded), (w2_sb, w2_hi, w2_loaded)):
                act.wait_ge(loaded, 32)
                for c, i in SPLIT12.items():
                    last = nc.scalar.copy(w_hi[:, i, :], w_sb[:, c, :])
                last.then_inc(w_rounded, 1)
            act.wait_ge(bias_loaded, 16)

            def round_group(n, g, rows, split):
                act.wait_ge(prod_ready, n + (g + 1))
                b = buffer(g + G0)
                nc.scalar.copy(prod_hi[0:rows, b, 0:split, :], prod[0:rows, b, 0:split, :]).then_inc(hi_ready, 1)

            def relu(out, acc_in, layer, rows):
                return nc.scalar.activation(out, acc_in, ACT.Relu, bias=bias[rows, layer:layer + 1])

            lower, upper = slice(0, HALF), slice(HALF, P)

            def evacuate0(n_contracted, tile_count):
                act.wait_ge(contracted, n_contracted)
                relu(x1[upper, :], acc[0][upper, :], 0, upper)
                relu(x1[lower, :], acc[0][upper, :], 0, upper).then_inc(x1_ready, 1)
                if not (isinstance(tile_count, int) and tile_count == 1):
                    act.wait_ge(sum01_done, tile_count - 1)
                relu(direct01[lower, :], acc[0][lower, :], 0, lower).then_inc(acc0_read, 1)

            def evacuate1(n_contracted):
                act.wait_ge(contracted, n_contracted)
                relu(x2[lower, :], acc[1][lower, :], 1, lower)
                relu(x2[upper, :], acc[1][lower, :], 1, lower).then_inc(x2_ready, 1)
                relu(direct01[upper, :], acc[1][upper, :], 1, upper).then_inc(acc1_read, 1)

            def evacuate2(n_contracted, t, first):
                act.wait_ge(contracted, n_contracted)
                if not first:
                    act.wait_ge(sum2_done, t)
                relu(direct2[:, :], acc[2][:, :], 2, slice(0, P)).then_inc(acc2_read, 1)

            for g, (_, _, split) in enumerate(GROUPS0):
                round_group(G0, g - G0, ROWS0, split)
            evacuate0(G0, 1)

            def tile(t, last_tile=False, first_tile=False):
                n = before(act, t)
                for g in range(G12):
                    round_group(n, g, P, GROUPS12[g][2])
                    if g == 1 and not first_tile:
                        evacuate2(n, t - 1, isinstance(t, int) and t == 1)
                g = G12
                if not last_tile:
                    round_group(n, g, ROWS0, GROUPS0[0][2])
                    evacuate1(n + G12)
                    round_group(n, g + 1, ROWS0, GROUPS0[1][2])
                    g += G0
                else:
                    evacuate1(n + G12)
                for i in range(G12):
                    round_group(n, g + i, P, GROUPS12[i][2])
                    if i == 1 and not last_tile:
                        evacuate0(n + (G12 + G0), t + 2)

            tile(0, first_tile=True)
            tile(1)
            with act.Fori(2, TILES - 1) as t:
                tile(t)
            tile(TILES - 1, last_tile=True)
            evacuate2(G0 + PER_TILE * TILES - G0, TILES - 1, False)

            act.wait_ge(mlp_loaded, 16 * 7)
            for m in range(H1 // P):
                act.wait_ge(h1_ready, m + 1)
                nc.scalar.activation(h1[:, m, :], acc_h1[:, m, :], ACT.Relu, bias=bt1_sb[:, m:m + 1]).then_inc(h1_relu, 1)
            for m in range(H2 // P):
                act.wait_ge(h2_ready, m + 1)
                nc.scalar.activation(h2[:, m, :], acc_h2[m][:, :], ACT.Relu, bias=bt2_sb[:, m:m + 1]).then_inc(h2_relu, 1)
            act.wait_ge(y_ready, 1)
            nc.scalar.copy(y_sb[:, :], acc_y[0:1, :]).then_inc(y_copied, 1)
            act.wait_ge(y_copied, 1)
            act.dma_start(y, y_sb[:, :]).then_inc(y_stored, 16)
            act.wait_ge(y_stored, 16)

        @block.vector
        def _(dve):
            dve.wait_ge(w0_loaded, 32)
            nc.vector.tensor_tensor(w0_sb[0:ROWS0], w0_sb[0:ROWS0], w0m_sb[0:ROWS0], ALU.add).then_inc(w0_added, 1)
            dve.wait_ge(w0_added, 1)

            def split_weights(layer):
                w_sb, w_hi, w_lo, index, rows = ((w0_sb, w0_hi, w0_lo, SPLIT0, ROWS0),
                                                 (w1_sb, w1_hi, w1_lo, SPLIT12, P),
                                                 (w2_sb, w2_hi, w2_lo, SPLIT12, P))[layer]
                dve.wait_ge(w_rounded, layer + 1)
                for c, i in index.items():
                    last = nc.vector.tensor_tensor(w_lo[0:rows, i, :], w_sb[0:rows, c, :],
                                                   w_hi[0:rows, i, :].bitcast(F32), ALU.subtract)
                last.then_inc(w_split, 1)

            def multiply(n, g, layer, i):
                c, k, _ = (GROUPS0 if layer == 0 else GROUPS12)[i]
                rows = ROWS0 if layer == 0 else P
                b = buffer(g + G0)
                x0 = x0_shifted if layer == 0 else x0_pairs
                xk = (x0_thrice, x1, x2)[layer]
                if not (isinstance(n, int) and n + g < RING):
                    dve.wait_ge(contracted, n + (g + 1 - RING))
                nc.vector.tensor_tensor(
                    prod[0:rows, b, 0:k, :], x0[0:rows, c:c + k, :],
                    xk[0:rows, :].rearrange("p (o n) -> p o n", o=1).to_broadcast([rows, k, N]),
                    ALU.mult).then_inc(prod_ready, 1)

            def rest(n, g, layer, i):
                split = (GROUPS0 if layer == 0 else GROUPS12)[i][2]
                rows = ROWS0 if layer == 0 else P
                b = buffer(g + G0)
                dve.wait_ge(hi_ready, n + (g + 1))
                nc.vector.tensor_tensor(prod_lo[0:rows, b, 0:split, :], prod[0:rows, b, 0:split, :],
                                        prod_hi[0:rows, b, 0:split, :].bitcast(F32),
                                        ALU.subtract).then_inc(lo_ready, 1)

            def columns(t):
                return slice(t * TB, (t + 1) * TB) if isinstance(t, int) else bass.ds(t * TB, TB)

            def sum01(t, count):
                dve.wait_ge(acc1_read, count)
                nc.vector.tensor_reduce(logits[:, 0, columns(t)],
                                        direct01[:, :].rearrange("p (b d) -> p b d", d=DIM),
                                        AX.X, ALU.add).then_inc(sum01_done, 1)

            def sum2(t, count):
                dve.wait_ge(acc2_read, count)
                nc.vector.tensor_reduce(logits[:, 1, columns(t)],
                                        direct2[:, :].rearrange("p (b d) -> p b d", d=DIM),
                                        AX.X, ALU.add).then_inc(sum2_done, 1)

            split_weights(0)
            dve.wait_ge(shifted_in, 16 * (OPC + 1))
            for i in range(G0):
                multiply(G0, i - G0, 0, i)
            split_weights(1)
            for i in range(G0):
                rest(G0, i - G0, 0, i)
            split_weights(2)

            def tile(t, first_tile=False, last_tile=False):
                n = before(dve, t)
                loads = 32 * (t + 1) if isinstance(t, int) else dve.snap(t * 32 + 32)
                loads0 = 64 * (t + 2) if isinstance(t, int) else dve.snap(t * 64 + 128)
                dve.wait_ge(x1_ready, t + 1)
                for i in range(G12):
                    dve.wait_ge(pairs_in[i], loads)
                    multiply(n, i, 1, i)
                    if i:
                        rest(n, i - 1, 1, i - 1)
                    elif not first_tile:
                        rest(n, -1, 2, G12 - 1)
                    if i == 2 and not first_tile:
                        sum2(t - 1, t)
                g = G12
                if not last_tile:
                    dve.wait_ge(shifted_in, loads0)
                    multiply(n, g, 0, 0)
                    rest(n, g - 1, 1, G12 - 1)
                    multiply(n, g + 1, 0, 1)
                    rest(n, g, 0, 0)
                    rest(n, g + 1, 0, 1)
                    g += G0
                else:
                    rest(n, g - 1, 1, G12 - 1)
                dve.wait_ge(x2_ready, t + 1)
                for i in range(G12):
                    multiply(n, g + i, 2, i)
                    if i:
                        rest(n, g + i - 1, 2, i - 1)
                    else:
                        sum01(t, t + 1)

            tile(0, first_tile=True)
            with dve.Fori(1, TILES - 1) as t:
                tile(t)
            tile(TILES - 1, last_tile=True)
            rest(before(dve, TILES - 1), 2 * G12 - 1, 2, G12 - 1)
            sum2(TILES - 1, TILES)

        @block.tensor
        def _(pe):
            def contract(n, g, layer, i):
                groups = GROUPS0 if layer == 0 else GROUPS12
                c0, k, split = groups[i]
                w_sb, w_hi, w_lo, index = ((w0_sb, w0_hi, w0_lo, SPLIT0), (w1_sb, w1_hi, w1_lo, SPLIT12),
                                           (w2_sb, w2_hi, w2_lo, SPLIT12))[layer]
                chunks = CHUNKS0 if layer == 0 else CHUNKS
                full, least = (ROWS0, LAST0) if layer == 0 else (P, HALF)
                b = buffer(g + G0)
                out = acc[layer][:, :]
                pe.wait_ge(prod_ready, n + (g + 1))
                for j in range(split, k):
                    rows = least if c0 + j == chunks - 1 else full
                    nc.tensor.matmul(out, w_sb[0:rows, c0 + j, :], prod[0:rows, b, j, :],
                                     start=(i == 0 and j == split), stop=False)
                pe.wait_ge(hi_ready, n + (g + 1))
                for j in range(split):
                    s = index[c0 + j]
                    nc.tensor.matmul(out, w_lo[0:full, s, :], prod_hi[0:full, b, j, :], start=False, stop=False)
                    nc.tensor.matmul(out, w_hi[0:full, s, :], prod_hi[0:full, b, j, :], start=False, stop=False)
                pe.wait_ge(lo_ready, n + (g + 1))
                for j in range(split):
                    s = index[c0 + j]
                    last = nc.tensor.matmul(out, w_hi[0:full, s, :], prod_lo[0:full, b, j, :], start=False,
                                            stop=(i == len(groups) - 1 and j == split - 1))
                last.then_inc(contracted, 1)

            pe.wait_ge(w_split, 1)
            for i in range(G0):
                contract(G0, i - G0, 0, i)
            pe.wait_ge(w_split, 3)

            def tile(t, last_tile=False):
                n = before(pe, t)
                first = isinstance(t, int) and t == 0
                if not first:
                    pe.wait_ge(acc1_read, t)
                for i in range(G12):
                    contract(n, i, 1, i)
                g = G12
                if not last_tile:
                    pe.wait_ge(acc0_read, t + 1)
                    for i in range(G0):
                        contract(n, g + i, 0, i)
                    g += G0
                if not first:
                    pe.wait_ge(acc2_read, t)
                for i in range(G12):
                    contract(n, g + i, 2, i)

            tile(0)
            with pe.Fori(1, TILES - 1) as t:
                tile(t)
            tile(TILES - 1, last_tile=True)

            pe.wait_ge(mlp_loaded, 16 * 7)
            pe.wait_ge(sum01_done, TILES)
            pe.wait_ge(sum2_done, TILES)
            for m in range(H1 // P):
                cols = slice(m * P, (m + 1) * P)
                for c in range(2):
                    nc.tensor.matmul(acc_h1[:, m, :], wt1_sb[:, c, cols], logits[:, c, :], start=(c == 0), stop=False)
                nc.tensor.matmul(acc_h1[:, m, :], wt1d_sb[:, cols], dense_sb[:, :], start=False, stop=True).then_inc(h1_ready, 1)
            pe.wait_ge(acc1_read, TILES)
            pe.wait_ge(acc2_read, TILES)
            for m in range(H2 // P):
                cols = slice(m * P, (m + 1) * P)
                for c in range(H1 // P):
                    if m == 0:
                        pe.wait_ge(h1_relu, c + 1)
                    last = nc.tensor.matmul(acc_h2[m][:, :], wt2_sb[:, c, cols], h1[:, c, :], start=(c == 0),
                                            stop=(c == H1 // P - 1))
                last.then_inc(h2_ready, 1)
            for c in range(H2 // P):
                pe.wait_ge(h2_relu, c + 1)
                last = nc.tensor.matmul(acc_y[0:1, :], wt3_sb[:, c:c + 1], h2[:, c, :], start=(c == 0),
                                        stop=(c == H2 // P - 1))
            last.then_inc(y_ready, 1)


def kernel(**inputs):
    import concourse.bacc as bacc
    from concourse.bass_utils import run_bass_kernel_spmd

    ins = {k: np.asarray(v) for k, v in inputs.items()}
    h = np.arange(FIELDS)
    pad = OPC * CHUNKS0 - OFFSETS
    w0 = ins["L0_rec_w0"]
    w0_rows = np.stack([w0[h, (h + o) % FIELDS] for o in range(OFFSETS)])
    w0_mirror = np.stack([w0[(h + o) % FIELDS, h] for o in range(1, OFFSETS)])
    w0_rows = np.pad(w0_rows, ((0, pad), (0, 0), (0, 0)))
    w0_mirror = np.pad(w0_mirror, ((1, pad), (0, 0), (0, 0)))
    order = np.r_[HALF:LAYER, 0:HALF]
    first_row = np.concatenate([[0], np.cumsum(VOCABS)[:-1]]).astype(np.int32)
    arrays = {
        "tables": np.concatenate([ins[f"tbl_{f}"] for f in range(FIELDS)], axis=0),
        "ids": ins["ids"].reshape(TILES, TB, FIELDS).transpose(0, 2, 1).reshape(TILES, FIELDS * TB),
        "field_base": np.repeat(first_row, TB).reshape(GP, GJ),
        "w0": w0_rows.reshape(-1, LAYER)[:, order],
        "w0_mirror": w0_mirror.reshape(-1, LAYER)[:, order],
        "w1": ins["L0_rec_w1"].reshape(-1, LAYER),
        "w2": ins["L0_rec_w2"].reshape(-1, LAYER),
        "cin_bias": np.stack([ins["L0_rec_b0"][order], ins["L0_rec_b1"], ins["L0_rec_b2"]], axis=1),
        "dense": ins["dense_ctx"].T,
        "wt1": ins["W_top1"], "bt1": ins["b_top1"].reshape(-1, P).T,
        "wt2": ins["W_top2"], "bt2": ins["b_top2"].reshape(-1, P).T,
        "wt3": ins["W_top3"].reshape(-1, P).T,
    }
    arrays = {k: np.ascontiguousarray(v) for k, v in arrays.items()}
    nc = bacc.Bacc("TRN2", target_bir_lowering=False, num_devices=1)
    aps = {k: nc.dram_tensor(k, v.shape, mybir.dt.from_np(v.dtype), kind="ExternalInput").ap()
           for k, v in arrays.items()}
    y = nc.dram_tensor("y", (1, BATCH), F32, kind="ExternalOutput").ap()
    build(nc, y=y, **aps)
    result = run_bass_kernel_spmd(nc, [arrays], core_ids=[0])
    return result.results[0]["y"].reshape(BATCH, 1)
```

```python
from contextlib import ExitStack

import numpy as np

import concourse.bass as bass
from concourse import mybir

F32 = mybir.dt.float32
F32R = mybir.dt.float32r
I32 = mybir.dt.int32
ALU = mybir.AluOpType
ACT = mybir.ActivationFunctionType
AX = mybir.AxisListType

P = 128
BATCH, FIELDS, DIM = 512, 39, 16
VOCABS = [125000, 1250, 1000, 1000, 1000, 1250, 12500, 1000, 1250, 12500, 1250, 125000, 1000, 1000,
          1000, 1250, 1250, 125000, 125000, 125000, 12500, 1000, 125000, 1250, 125000, 125000,
          125000, 12500, 12500, 125000, 125000, 1000, 1000, 12500, 125000, 125000, 125000, 1000, 1250]
LAYER = 128
HALF = LAYER // 2
N = 512
TB = N // DIM
TILES = BATCH // TB
OFFSETS = FIELDS // 2 + 1
OPC = P // FIELDS
ROWS0 = OPC * FIELDS
CHUNKS0 = -(-OFFSETS // OPC)
LAST0 = (OFFSETS - OPC * (CHUNKS0 - 1)) * FIELDS
CHUNKS = -(-FIELDS // 2)
X0_ROWS = FIELDS + OPC * CHUNKS0 - 1
GJ = -(-FIELDS * TB // P)
FULL_GP, REST_GJ = divmod(FIELDS * TB, GJ)
REPEAT_GP = (X0_ROWS - FIELDS) * TB // GJ
assert REPEAT_GP * GJ == (X0_ROWS - FIELDS) * TB

GROUPS = [[("s", 0, 2), ("s", 2, 2), ("p", 6, 1), ("s", 4, 2)],
          [("s", 0, 2), ("p", 2, 2), ("s", 4, 2), ("p", 6, 2), ("s", 8, 2), ("s", 10, 2),
           ("p", 12, 2), ("s", 14, 2), ("p", 18, 2), ("s", 16, 2)],
          [("s", 0, 2), ("p", 2, 2), ("s", 4, 2), ("p", 6, 2), ("s", 8, 2), ("p", 10, 2),
           ("s", 12, 2), ("p", 14, 2), ("p", 18, 2), ("s", 16, 2)]]
QUAD = 4
QUADS = CHUNKS // QUAD
WIDE = 2


def of_kind(kind, layer):
    return [(c, k) for what, c, k in GROUPS[layer] if what == kind]


S = [len(of_kind("s", layer)) for layer in range(3)]
PL = [len(of_kind("p", layer)) for layer in range(3)]
S_TILE, P_TILE = sum(S), sum(PL)
SPLIT_RING = 4
PSUM_RING = 2
PLAIN_RING = 5
assert P_TILE % PLAIN_RING == 0
assert 2 * S_TILE % SPLIT_RING == 0 and S_TILE % PSUM_RING == 0
H1, H2 = 512, 256


def build(nc, tables, ids, field_base, w0, w0_mirror, w1, w2, cin_bias, dense, wt1, bt1, wt2, bt2,
          wt3, y):
    x0_dram = nc.dram_tensor("x0_scratch", (TILES, X0_ROWS, N), F32, kind="Internal").ap()

    with ExitStack() as ctx:
        def sb(name, shape, dt=F32):
            return ctx.enter_context(nc.sbuf_tensor(name, shape, dt))

        def sem(name):
            return ctx.enter_context(nc.semaphore(name))

        ids_sb = sb("ids_sb", [P, TILES, GJ], I32)
        base_sb = sb("base_sb", [P, GJ], I32)
        rows_now = sb("rows_now", [P, 2, GJ], I32)
        gathered = sb("gathered", [P, 2, GJ * DIM])
        x0_pairs = sb("x0_pairs", [P, 2, CHUNKS, N])
        x0_shifted = sb("x0_shifted", [P, CHUNKS0, N])
        x0_thrice = sb("x0_thrice", [P, N])
        xk_sb = sb("xk_sb", [P, 2, N])
        direct01 = sb("direct01", [P, N])
        direct2 = sb("direct2", [P, N])
        plain = sb("plain", [P, PLAIN_RING, WIDE, N])
        prod_hi = sb("prod_hi", [P, SPLIT_RING, WIDE, N], F32R)
        prod_lo = sb("prod_lo", [P, SPLIT_RING, WIDE, N], F32R)
        staging = x0_pairs[:, 1].rearrange("p c (q s) -> p (c q) s", s=LAYER)
        w_sb = [staging[:, 0:CHUNKS0, :], staging[:, CHUNKS0:CHUNKS0 + CHUNKS, :],
                staging[:, CHUNKS0 + CHUNKS:CHUNKS0 + 2 * CHUNKS, :]]
        w0m_sb = staging[:, CHUNKS0 + 2 * CHUNKS:2 * CHUNKS0 + 2 * CHUNKS, :]
        w_plain = [sb(f"w{i}_plain", [P, PL[i], WIDE, LAYER]) for i in range(3)]
        w_hi = [sb(f"w{i}_hi", [P, S[i], WIDE, LAYER], F32R) for i in range(3)]
        w_lo = [sb(f"w{i}_lo", [P, S[i], WIDE, LAYER], F32R) for i in range(3)]
        bias = sb("bias", [P, 3])
        logits = sb("logits", [P, 2, BATCH])
        late = x0_shifted[:, :, :].rearrange("p c n -> p (c n)")
        wt1_sb = late[:, 0:2 * H1].rearrange("p (c n) -> p c n", n=H1)
        wt2_sb = late[:, 2 * H1:2 * H1 + H1 // P * H2].rearrange("p (c n) -> p c n", n=H2)
        wt1d_sb = late[0:DIM, 4 * H1:5 * H1]
        dense_sb = late[0:DIM, 5 * H1:5 * H1 + BATCH]
        wt3_sb = sb("wt3_sb", [P, H2 // P])
        bt1_sb = sb("bt1_sb", [P, H1 // P])
        bt2_sb = sb("bt2_sb", [P, H2 // P])
        y_sb = sb("y_sb", [1, BATCH])

        acc = [ctx.enter_context(nc.psum_tensor(f"acc{i}", [P, N], F32)) for i in range(2)]
        xk_ps = [ctx.enter_context(nc.psum_tensor(f"xk_ps{i}", [P, N], F32)) for i in range(2)]
        split = ctx.enter_context(nc.psum_tensor("split", [P, PSUM_RING, WIDE, N], F32))
        h1 = plain[:, 0:2].rearrange("p a b n -> p (a b) n")
        h2 = plain[:, 2]
        acc_h1 = split[:, :].rearrange("p a b n -> p (a b) n")
        acc_h2 = acc
        acc_y = xk_ps[0]

        ids_loaded = sem("ids_loaded")
        w0_loaded, w1_loaded, w2_loaded = sem("w0_loaded"), sem("w1_loaded"), sem("w2_loaded")
        bias_loaded, mlp_loaded = sem("bias_loaded"), sem("mlp_loaded")
        row_numbers = sem("row_numbers")
        rows_in = [sem(f"rows_in{i}") for i in range(2)]
        x0_stored = [sem(f"x0_stored{i}") for i in range(2)]
        shifted_in = sem("shifted_in")
        quad_in = [[sem(f"quad_in{parity}{q}") for q in range(QUADS)] for parity in range(2)]
        w0_added = sem("w0_added")
        w_rounded = sem("w_rounded")
        w_split = sem("w_split")
        split_ready, hi_ready, lo_ready, split_used = (
            sem("split_ready"), sem("hi_ready"), sem("lo_ready"), sem("split_used"))
        plain_ready, plain_used = sem("plain_ready"), sem("plain_used")
        acc_read = [sem(f"acc{i}_read") for i in range(3)]
        xk_in_psum = [sem(f"xk{i}_in_psum") for i in range(3)]
        xk_in_sbuf = [None, sem("xk1_in_sbuf"), sem("xk2_in_sbuf")]
        direct01_free, direct2_free = sem("direct01_free"), sem("direct2_free")
        h1_ready, h1_relu, h2_ready, h2_relu = sem("h1_ready"), sem("h1_relu"), sem("h2_ready"), sem("h2_relu")
        y_ready, y_copied, y_stored = sem("y_ready"), sem("y_copied"), sem("y_stored")

        def at(eng, t, per_tile, start=0):
            return start + per_tile * t if isinstance(t, int) else eng.snap(t * per_tile + start)

        def all_tiles(eng, tile):
            tile(0, 0, 0)
            with eng.Fori(0, (TILES - 2) // 2) as turn:
                for i in (1, 2):
                    tile(eng.snap(turn * 2 + i), i % 2, eng.snap(turn + i // 2))
            tile(TILES - 1, (TILES - 1) % 2, (TILES - 1) // 2)

        def is_last(t):
            return isinstance(t, int) and t == TILES - 1

        def rows_of(layer):
            return ROWS0 if layer == 0 else P

        def over_chunks(xk, k):
            return xk.rearrange("p (o n) -> p o n", o=1).to_broadcast([xk.shape[0], k, N])

        def split_buffer(g, parity):
            return (S[0] + g + parity * S_TILE) % SPLIT_RING

        def psum_buffer(g):
            return (S[0] + g) % PSUM_RING

        def plain_buffer(g):
            return (PL[0] + g) % PLAIN_RING

        SHIFTED_INC = 16 * (OPC + 1)
        QUAD_INC = 16 * 2
        STORED_INC = 16 * 3

        block = ctx.enter_context(nc.Block())

        @block.sync
        def _(sp):
            sp.dma_start(ids_sb[:, :, :], ids.rearrange("t (p j) -> p t j", j=GJ)).then_inc(ids_loaded, 16)
            sp.dma_start(base_sb[:, :], field_base).then_inc(ids_loaded, 16)

            def load_shifted(t):
                a = x0_dram[t, 0]
                sp.dma_start(x0_thrice[0:ROWS0, :],
                             bass.AP(tensor=a.tensor, offset=a.offset, ap=[[0, OPC], [N, FIELDS], [1, N]])
                             ).then_inc(shifted_in, 16)
                for o in range(OPC):
                    sp.dma_start(x0_shifted[o * FIELDS:(o + 1) * FIELDS, :, :],
                                 bass.AP(tensor=a.tensor, offset=a.offset + o * N,
                                         ap=[[N, FIELDS], [OPC * N, CHUNKS0], [1, N]])
                                 ).then_inc(shifted_in, 16)

            def store(t, odd, half):
                sp.wait_ge(rows_in[odd], at(sp, half, 16 * GJ, 16 * GJ))
                a = x0_dram[t, 0]
                m = GJ * DIM
                for first, parts, width, to in ((0, FULL_GP, m, 0), (FULL_GP, 1, REST_GJ * DIM, FULL_GP * m),
                                                (0, REPEAT_GP, m, FIELDS * N)):
                    sp.dma_start(bass.AP(tensor=a.tensor, offset=a.offset + to, ap=[[m, parts], [1, width]]),
                                 gathered[first:first + parts, odd, 0:width]).then_inc(x0_stored[odd], 16)

            def load_quad(t, parity, q):
                c = QUAD * q
                a = x0_dram[t, 0]
                for i in range(2):
                    sp.dma_start(x0_pairs[i * HALF:(i + 1) * HALF, parity, c:c + QUAD, :],
                                 bass.AP(tensor=a.tensor, offset=a.offset + (2 * c + i) * N,
                                         ap=[[0, HALF], [2 * N, QUAD], [1, N]])
                                 ).then_inc(quad_in[parity][q], 16)

            store(0, 0, 0)
            sp.wait_ge(x0_stored[0], STORED_INC)
            load_shifted(0)
            for q in range(QUADS):
                load_quad(0, 0, q)
            store(1, 1, 0)
            sp.wait_ge(split_used, S[0])
            sp.wait_ge(x0_stored[1], STORED_INC)
            load_shifted(1)

            sp.wait_ge(w_split, 3)
            with sp.Fori(0, (TILES - 2) // 2) as turn:
                for i in range(2):
                    t, following, after_next = (sp.snap(turn * 2 + (i + n)) for n in range(3))
                    s = at(sp, t, S_TILE, S[0])
                    sp.wait_ge(split_used, s)
                    for q in range(QUADS - 1):
                        load_quad(following, 1 - i, q)
                    store(after_next, i, sp.snap(turn + 1))
                    sp.wait_ge(x0_stored[i], at(sp, turn, STORED_INC, 2 * STORED_INC))
                    load_quad(following, 1 - i, QUADS - 1)
                    sp.wait_ge(split_used, s + (S[1] + S[0]))
                    load_shifted(after_next)
            sp.wait_ge(split_used, S[0] + S_TILE * (TILES - 2))
            for q in range(QUADS):
                load_quad(TILES - 1, (TILES - 1) % 2, q)

        @block.gpsimd
        def _(pool):
            pool.wait_ge(ids_loaded, 32)

            def number_rows(t, odd):
                pool.tensor_tensor(rows_now[:, odd, :],
                                   ids_sb[:, t, :] if isinstance(t, int) else
                                   ids_sb[:, bass.ds(t, 1), :].rearrange("p o j -> p (o j)"),
                                   base_sb[:, :], ALU.add).then_inc(row_numbers, 1)
                pool.wait_ge(row_numbers, 1)

            def gather(odd, j):
                pool.indirect_dma_start(
                    gathered[:, odd, j * DIM:(j + 1) * DIM], None, tables,
                    bass.IndirectOffsetOnAxis(ap=rows_now[:, odd, j:j + 1], axis=0)
                ).then_inc(rows_in[odd], 16)

            def multiply(layer, i, g, parity):
                c, k = of_kind("p", layer)[i]
                rows = rows_of(layer)
                x0 = x0_shifted if layer == 0 else x0_pairs[:, parity]
                xk = x0_thrice[0:rows, :] if layer == 0 else xk_sb[:, parity, :]
                nc.gpsimd.tensor_tensor(plain[0:rows, plain_buffer(g), 0:k, :], x0[0:rows, c:c + k, :],
                                        over_chunks(xk, k), ALU.mult).then_inc(plain_ready, 1)

            def gather_tile(t):
                number_rows(t, t % 2)
                pool.sem_clear(row_numbers)
                for j in range(GJ):
                    gather(t % 2, j)

            gather_tile(0)
            gather_tile(1)
            pool.wait_ge(shifted_in, SHIFTED_INC)
            for i in range(PL[0]):
                multiply(0, i, i - PL[0], 0)
            pool.wait_ge(x0_stored[0], STORED_INC)
            gather_tile(2)

            def tile(t, parity, half):
                p = at(pool, t, P_TILE, PL[0])
                quads = at(pool, half, QUAD_INC, QUAD_INC)
                shifted = at(pool, t, SHIFTED_INC, 2 * SHIFTED_INC)
                ahead, odd = 3, 1 - parity
                gathers = 0 if isinstance(t, int) and t + ahead >= TILES else GJ
                stored = at(pool, half, STORED_INC, STORED_INC * (1 + parity))
                steps = [(1, i) for i in range(PL[1])]
                if not is_last(t):
                    steps += [(0, i) for i in range(PL[0])]
                steps += [(2, i) for i in range(PL[2])]
                for n, (layer, i) in enumerate(steps):
                    if layer and not i:
                        pool.wait_ge(xk_in_sbuf[layer], t + 1)
                    if layer == 1:
                        pool.wait_ge(quad_in[parity][of_kind("p", 1)[i][0] // QUAD], quads)
                    if layer == 0 and not i:
                        pool.wait_ge(shifted_in, shifted)
                    if not (isinstance(p, int) and p + n < PLAIN_RING):
                        pool.wait_ge(plain_used, p + (n + 1 - PLAIN_RING))
                    multiply(layer, i, n, parity)
                    for j in range(gathers * n // len(steps), gathers * (n + 1) // len(steps)):
                        if not j:
                            pool.wait_ge(x0_stored[odd], stored)
                            number_rows(at(pool, t, 1, ahead), odd)
                            pool.sem_clear(row_numbers)
                        gather(odd, j)

            tile(0, 0, 0)
            with pool.Fori(0, (TILES - 4) // 2) as turn:
                for i in (1, 2):
                    tile(pool.snap(turn * 2 + i), i % 2, pool.snap(turn + i // 2))
            for t in range(TILES - 3, TILES):
                tile(t, t % 2, t // 2)

        @block.scalar
        def _(act):
            def load(out, source, loaded):
                act.dma_start(out, source).then_inc(loaded, 16)

            def load_weights(layer, w, loaded):
                whole = (CHUNKS - 1) * P
                load(w_sb[layer][:, 0:CHUNKS - 1, :], w[0:whole, :].rearrange("(c p) s -> p c s", p=P), loaded)
                load(w_sb[layer][0:HALF, CHUNKS - 1, :], w[whole:, :], loaded)

            load(w_sb[0][0:ROWS0, :, :], w0.rearrange("(c p) s -> p c s", p=ROWS0), w0_loaded)
            load(w0m_sb[0:ROWS0, :, :], w0_mirror.rearrange("(c p) s -> p c s", p=ROWS0), w0_loaded)
            load(bias[:, :], cin_bias, bias_loaded)
            load_weights(1, w1, w1_loaded)
            load_weights(2, w2, w2_loaded)

            def round_weights(layer):
                rows = rows_of(layer)
                for i, (c, k) in enumerate(of_kind("p", layer) if layer else ()):
                    for j in range(k):
                        r = HALF if c + j == CHUNKS - 1 else P
                        nc.scalar.copy(w_plain[layer][0:r, i, j, :], w_sb[layer][0:r, c + j, :])
                for i, (c, k) in enumerate(of_kind("s", layer)):
                    last = nc.scalar.copy(w_hi[layer][0:rows, i, 0:k, :], w_sb[layer][0:rows, c:c + k, :])
                last.then_inc(w_rounded, 1)

            act.wait_ge(w0_added, 1)
            round_weights(0)
            act.wait_ge(w1_loaded, 32)
            round_weights(1)
            act.wait_ge(w2_loaded, 32)
            round_weights(2)
            act.wait_ge(bias_loaded, 16)

            def round_group(layer, i, s, g, parity):
                rows, k = rows_of(layer), of_kind("s", layer)[i][1]
                buf = split_buffer(g, parity)
                act.wait_ge(split_ready, s + (g + 1))
                if not (isinstance(s, int) and s + g < SPLIT_RING):
                    act.wait_ge(split_used, s + (g + 1 - SPLIT_RING))
                nc.scalar.copy(prod_hi[0:rows, buf, 0:k, :],
                               split[0:rows, psum_buffer(g), 0:k, :]).then_inc(hi_ready, 1)

            lower, upper = slice(0, HALF), slice(HALF, P)

            def relu(out, acc_in, layer, rows):
                return nc.scalar.activation(out, acc_in, ACT.Relu, bias=bias[rows, layer:layer + 1])

            def evacuate(layer, t, parity, used):
                direct, feeding = (lower, upper) if layer == 0 else (upper, lower)
                z = acc[parity]
                act.wait_ge(split_used, used)
                relu(xk_sb[lower, parity, :], z[feeding, :], layer, feeding)
                relu(xk_sb[upper, parity, :], z[feeding, :], layer, feeding).then_inc(xk_in_sbuf[layer + 1], 1)
                act.wait_ge(xk_in_sbuf[layer + 1], t + 1)
                nc.scalar.copy(xk_ps[parity][:, :], xk_sb[:, parity, :]).then_inc(xk_in_psum[layer + 1], 1)
                if layer == 0:
                    act.wait_ge(direct01_free, t + 1)
                relu(direct01[direct, :], z[direct, :], layer, direct).then_inc(acc_read[layer], 1)

            def evacuate2(t, parity, used):
                act.wait_ge(split_used, used)
                act.wait_ge(direct2_free, t + 1)
                relu(direct2[:, :], acc[parity][:, :], 2, slice(0, P)).then_inc(acc_read[2], 1)

            def x0_to_psum(parity, loads):
                act.wait_ge(shifted_in, loads)
                nc.scalar.copy(xk_ps[parity][0:ROWS0, :], x0_thrice[0:ROWS0, :]).then_inc(xk_in_psum[0], 1)

            x0_to_psum(0, SHIFTED_INC)
            for i in range(S[0]):
                round_group(0, i, S[0], i - S[0], 0)
            evacuate(0, 0, 0, S[0])

            def tile(t, parity, half):
                s = at(act, t, S_TILE, S[0])
                shifted = at(act, t, SHIFTED_INC, 2 * SHIFTED_INC)
                before = (t - 1) if isinstance(t, int) else act.snap(t - 1)
                if is_last(t):
                    for out, source in ((dense_sb, dense), (wt1d_sb, wt1[2 * P:, :]),
                                        (wt1_sb, wt1[0:2 * P, :].rearrange("(c p) n -> p c n", p=P)),
                                        (wt2_sb, wt2.rearrange("(c p) n -> p c n", p=P)),
                                        (wt3_sb[:, :], wt3), (bt1_sb[:, :], bt1), (bt2_sb[:, :], bt2)):
                        load(out, source, mlp_loaded)
                for i in range(S[1]):
                    round_group(1, i, s, i, parity)
                    if i == 1 and not (isinstance(t, int) and t == 0):
                        evacuate2(before, 1 - parity, s)
                    if i == S[1] - 2 and not is_last(t):
                        x0_to_psum(1 - parity, shifted)
                g = S[1]
                if not is_last(t):
                    for i in range(S[0]):
                        round_group(0, i, s, g + i, parity)
                    g += S[0]
                evacuate(1, t, parity, s + S[1])
                for i in range(S[2]):
                    round_group(2, i, s, g + i, parity)
                    if i == 1 and not is_last(t):
                        evacuate(0, t + 1 if isinstance(t, int) else act.snap(t + 1), 1 - parity,
                                 s + (S[1] + S[0]))

            all_tiles(act, tile)
            evacuate2(TILES - 1, (TILES - 1) % 2, S_TILE * TILES)

            act.wait_ge(mlp_loaded, 16 * 7)
            for m in range(H1 // P):
                act.wait_ge(h1_ready, m + 1)
                nc.scalar.activation(h1[:, m, :], acc_h1[:, m, :], ACT.Relu, bias=bt1_sb[:, m:m + 1]).then_inc(h1_relu, 1)
            for m in range(H2 // P):
                act.wait_ge(h2_ready, m + 1)
                nc.scalar.activation(h2[:, m, :], acc_h2[m][:, :], ACT.Relu, bias=bt2_sb[:, m:m + 1]).then_inc(h2_relu, 1)
            act.wait_ge(y_ready, 1)
            nc.scalar.copy(y_sb[:, :], acc_y[0:1, :]).then_inc(y_copied, 1)
            act.wait_ge(y_copied, 1)
            act.dma_start(y, y_sb[:, :]).then_inc(y_stored, 16)
            act.wait_ge(y_stored, 16)

        @block.vector
        def _(dve):
            dve.sem_inc(direct01_free, 1)
            dve.sem_inc(direct2_free, 1)
            dve.wait_ge(w0_loaded, 32)
            for kind in "ps":
                for i, (c, k) in enumerate(of_kind(kind, 0)):
                    out = w_plain[0][0:ROWS0, i, 0:k, :] if kind == "p" else w_sb[0][0:ROWS0, c:c + k, :]
                    last = nc.vector.tensor_tensor(out, w_sb[0][0:ROWS0, c:c + k, :], w0m_sb[0:ROWS0, c:c + k, :], ALU.add)
            last.then_inc(w0_added, 1)
            dve.wait_ge(w0_added, 1)

            def split_weights(layer):
                rows = rows_of(layer)
                dve.wait_ge(w_rounded, layer + 1)
                for i, (c, k) in enumerate(of_kind("s", layer)):
                    last = nc.vector.tensor_tensor(w_lo[layer][0:rows, i, 0:k, :], w_sb[layer][0:rows, c:c + k, :],
                                                   w_hi[layer][0:rows, i, 0:k, :].bitcast(F32), ALU.subtract)
                last.then_inc(w_split, 1)

            def multiply(layer, i, s, g, parity):
                c, k = of_kind("s", layer)[i]
                rows = rows_of(layer)
                x0 = x0_shifted if layer == 0 else x0_pairs[:, parity]
                if not (isinstance(s, int) and s + g < PSUM_RING):
                    dve.wait_ge(lo_ready, s + (g + 1 - PSUM_RING))
                nc.vector.tensor_tensor(split[0:rows, psum_buffer(g), 0:k, :], x0[0:rows, c:c + k, :],
                                        over_chunks(xk_ps[parity][0:rows, :], k), ALU.mult).then_inc(split_ready, 1)

            def rest(layer, i, s, g, parity):
                k = of_kind("s", layer)[i][1]
                rows = rows_of(layer)
                buf = split_buffer(g, parity)
                dve.wait_ge(hi_ready, s + (g + 1))
                nc.vector.tensor_tensor(prod_lo[0:rows, buf, 0:k, :], split[0:rows, psum_buffer(g), 0:k, :],
                                        prod_hi[0:rows, buf, 0:k, :].bitcast(F32),
                                        ALU.subtract).then_inc(lo_ready, 1)

            def sum_over_d(which, direct, t, ready, count, free):
                dve.wait_ge(ready, count)
                columns = slice(t * TB, (t + 1) * TB) if isinstance(t, int) else bass.ds(t * TB, TB)
                nc.vector.tensor_reduce(logits[:, which, columns],
                                        direct[:, :].rearrange("p (b d) -> p b d", d=DIM),
                                        AX.X, ALU.add).then_inc(free, 1)

            for layer in range(3):
                split_weights(layer)
            dve.wait_ge(xk_in_psum[0], 1)
            for i in range(S[0]):
                multiply(0, i, S[0], i - S[0], 0)
                if i:
                    rest(0, i - 1, S[0], i - 1 - S[0], 0)
            rest(0, S[0] - 1, S[0], -1, 0)

            def tile(t, parity, half):
                s = at(dve, t, S_TILE, S[0])
                quads = at(dve, half, QUAD_INC, QUAD_INC)
                first = isinstance(t, int) and t == 0
                dve.wait_ge(xk_in_psum[1], t + 1)
                for i in range(S[1]):
                    dve.wait_ge(quad_in[parity][of_kind("s", 1)[i][0] // QUAD], quads)
                    multiply(1, i, s, i, parity)
                    if i:
                        rest(1, i - 1, s, i - 1, parity)
                    elif not first:
                        rest(2, S[2] - 1, s, -1, parity)
                    if i == 3 and not first:
                        sum_over_d(1, direct2, t - 1 if isinstance(t, int) else dve.snap(t - 1),
                                   acc_read[2], t, direct2_free)
                g = S[1]
                if not is_last(t):
                    dve.wait_ge(xk_in_psum[0], t + 2)
                    multiply(0, 0, s, g, 1 - parity)
                    rest(1, S[1] - 1, s, g - 1, parity)
                    for i in range(1, S[0]):
                        multiply(0, i, s, g + i, 1 - parity)
                        rest(0, i - 1, s, g + i - 1, parity)
                    rest(0, S[0] - 1, s, g + S[0] - 1, parity)
                    g += S[0]
                else:
                    rest(1, S[1] - 1, s, g - 1, parity)
                dve.wait_ge(xk_in_psum[2], t + 1)
                for i in range(S[2]):
                    multiply(2, i, s, g + i, parity)
                    if i:
                        rest(2, i - 1, s, g + i - 1, parity)
                    else:
                        sum_over_d(0, direct01, t, acc_read[1], t + 1, direct01_free)

            all_tiles(dve, tile)
            last = TILES - 1
            rest(2, S[2] - 1, S[0] + S_TILE * last, S[1] + S[2] - 1, last % 2)
            sum_over_d(1, direct2, last, acc_read[2], TILES, direct2_free)

        @block.tensor
        def _(pe):
            def contract(layer, parity, s, s_before, p, p_before, z_parity):
                i = {"s": 0, "p": 0}
                out = acc[z_parity][:, :]
                full = rows_of(layer)
                chunks, least = (CHUNKS0, LAST0) if layer == 0 else (CHUNKS, HALF)
                start = True
                for n, (kind, c, k) in enumerate(GROUPS[layer]):
                    g = i[kind]
                    i[kind] += 1
                    if kind == "p":
                        slot = plain_buffer(p_before + g)
                        pe.wait_ge(plain_ready, p + (p_before + g + 1))
                        for j in range(k):
                            rows = least if c + j == chunks - 1 else full
                            last = nc.tensor.matmul(out, w_plain[layer][0:rows, g, j, :], plain[0:rows, slot, j, :],
                                                    start=start, stop=False)
                            start = False
                        last.then_inc(plain_used, 1)
                    else:
                        buf = split_buffer(s_before + g, parity)
                        pe.wait_ge(hi_ready, s + (s_before + g + 1))
                        for j in range(k):
                            for w in (w_lo, w_hi):
                                nc.tensor.matmul(out, w[layer][0:full, g, j, :], prod_hi[0:full, buf, j, :],
                                                 start=start, stop=False)
                                start = False
                        pe.wait_ge(lo_ready, s + (s_before + g + 1))
                        for j in range(k):
                            last = nc.tensor.matmul(out, w_hi[layer][0:full, g, j, :], prod_lo[0:full, buf, j, :],
                                                    start=False, stop=(n == len(GROUPS[layer]) - 1 and j == k - 1))
                        last.then_inc(split_used, 1)

            pe.wait_ge(w_split, 1)
            contract(0, 0, S[0], -S[0], PL[0], -PL[0], 0)

            def tile(t, parity, half):
                s, p = at(pe, t, S_TILE, S[0]), at(pe, t, P_TILE, PL[0])
                first = isinstance(t, int) and t == 0
                if first:
                    pe.wait_ge(w_split, 2)
                pe.wait_ge(acc_read[0], t + 1)
                contract(1, parity, s, 0, p, 0, parity)
                s_before, p_before = S[1], PL[1]
                if not is_last(t):
                    if not first:
                        pe.wait_ge(acc_read[2], t)
                    contract(0, parity, s, s_before, p, p_before, 1 - parity)
                    s_before, p_before = s_before + S[0], p_before + PL[0]
                if first:
                    pe.wait_ge(w_split, 3)
                pe.wait_ge(acc_read[1], t + 1)
                contract(2, parity, s, s_before, p, p_before, parity)

            all_tiles(pe, tile)

            pe.wait_ge(mlp_loaded, 16 * 7)
            pe.wait_ge(direct01_free, TILES + 1)
            pe.wait_ge(direct2_free, TILES + 1)
            for m in range(H1 // P):
                cols = slice(m * P, (m + 1) * P)
                for c in range(2):
                    nc.tensor.matmul(acc_h1[:, m, :], wt1_sb[:, c, cols], logits[:, c, :], start=(c == 0), stop=False)
                nc.tensor.matmul(acc_h1[:, m, :], wt1d_sb[:, cols], dense_sb, start=False, stop=True).then_inc(h1_ready, 1)
            for m in range(H2 // P):
                cols = slice(m * P, (m + 1) * P)
                for c in range(H1 // P):
                    if m == 0:
                        pe.wait_ge(h1_relu, c + 1)
                    last = nc.tensor.matmul(acc_h2[m][:, :], wt2_sb[:, c, cols], h1[:, c, :], start=(c == 0),
                                            stop=(c == H1 // P - 1))
                last.then_inc(h2_ready, 1)
            for c in range(H2 // P):
                pe.wait_ge(h2_relu, c + 1)
                last = nc.tensor.matmul(acc_y[0:1, :], wt3_sb[:, c:c + 1], h2[:, c, :], start=(c == 0),
                                        stop=(c == H2 // P - 1))
            last.then_inc(y_ready, 1)


def kernel(**inputs):
    import concourse.bacc as bacc
    from concourse.bass_utils import run_bass_kernel_spmd

    ins = {k: np.asarray(v) for k, v in inputs.items()}
    h = np.arange(FIELDS)
    pad = OPC * CHUNKS0 - OFFSETS
    w0 = ins["L0_rec_w0"]
    w0_rows = np.stack([w0[h, (h + o) % FIELDS] for o in range(OFFSETS)])
    w0_mirror = np.stack([w0[(h + o) % FIELDS, h] for o in range(1, OFFSETS)])
    w0_rows = np.pad(w0_rows, ((0, pad), (0, 0), (0, 0)))
    w0_mirror = np.pad(w0_mirror, ((1, pad), (0, 0), (0, 0)))
    order = np.r_[HALF:LAYER, 0:HALF]
    first_row = np.concatenate([[0], np.cumsum(VOCABS)[:-1]]).astype(np.int32)
    ids = ins["ids"].reshape(TILES, TB, FIELDS).transpose(0, 2, 1)
    arrays = {
        "tables": np.concatenate([ins[f"tbl_{f}"] for f in range(FIELDS)], axis=0),
        "ids": np.concatenate([ids, ids[:, 0:1]], axis=1).reshape(TILES, P * GJ),
        "field_base": np.repeat(np.append(first_row, first_row[0]), TB).reshape(P, GJ),
        "w0": w0_rows.reshape(-1, LAYER)[:, order],
        "w0_mirror": w0_mirror.reshape(-1, LAYER)[:, order],
        "w1": ins["L0_rec_w1"].reshape(-1, LAYER),
        "w2": ins["L0_rec_w2"].reshape(-1, LAYER),
        "cin_bias": np.stack([ins["L0_rec_b0"][order], ins["L0_rec_b1"], ins["L0_rec_b2"]], axis=1),
        "dense": ins["dense_ctx"].T,
        "wt1": ins["W_top1"], "bt1": ins["b_top1"].reshape(-1, P).T,
        "wt2": ins["W_top2"], "bt2": ins["b_top2"].reshape(-1, P).T,
        "wt3": ins["W_top3"].reshape(-1, P).T,
    }
    arrays = {k: np.ascontiguousarray(v) for k, v in arrays.items()}
    nc = bacc.Bacc("TRN2", target_bir_lowering=False, num_devices=1)
    aps = {k: nc.dram_tensor(k, v.shape, mybir.dt.from_np(v.dtype), kind="ExternalInput").ap()
           for k, v in arrays.items()}
    y = nc.dram_tensor("y", (1, BATCH), F32, kind="ExternalOutput").ap()
    build(nc, y=y, **aps)
    result = run_bass_kernel_spmd(nc, [arrays], core_ids=[0])
    return result.results[0]["y"].reshape(BATCH, 1)
```
